# Optimizing a Trainium2 kernel written in Bass

```python
import numpy as np
import jax
import jax.numpy as jnp

def _softmax(x, axis=-1):
    return jax.nn.softmax(x, axis=axis)

def _gelu(x):
    return jax.nn.gelu(x, approximate=True)

def _silu(x):
    return jax.nn.silu(x)

def _sigmoid(x):
    return jax.nn.sigmoid(x)

def _layernorm(x, axis=-1, eps=1e-05):
    m = jnp.mean(x, axis=axis, keepdims=True)
    v = jnp.var(x, axis=axis, keepdims=True)
    return (x - m) / jnp.sqrt(v + eps)

def _scatter_add(tgt, idx, src, axis=0):
    return tgt.at[idx].add(src)

def _segment_sum(src, seg, n):
    return jax.ops.segment_sum(src, seg, n)
kernel_name = 'mk_hybrid_d1_jaxref_r8_883c7c'

def setup_inputs(seed: int=0):
    np.random.seed(seed)
    _w = jnp.asarray

    def _L0_attn_a_setup():
        import jax, jax.numpy as jnp
        import numpy as np
        E = 128
        D = 64
        H = E // D
        EPS = 1e-05
        key = jax.random.key(seed)
        ks = jax.random.split(key, 8)
        std = 0.02
        x = jax.random.normal(ks[0], (2, 128, E), jnp.float32)
        Wq = jax.random.normal(ks[1], (E, E), jnp.float32) * std
        Wk = jax.random.normal(ks[2], (E, E), jnp.float32) * std
        Wv = jax.random.normal(ks[3], (E, E), jnp.float32) * std
        Wo = jax.random.normal(ks[4], (E, E), jnp.float32) * std
        delta = jnp.full((E,), float(np.log(0.99 / 0.01)), jnp.float32)
        G1 = jax.random.normal(ks[5], (E, D), jnp.float32) * std
        G2 = jax.random.normal(ks[6], (D, E), jnp.float32) * std
        norm_w = jnp.ones((E,), jnp.float32)
        return {'x': x, 'Wq': Wq, 'Wk': Wk, 'Wv': Wv, 'Wo': Wo, 'delta': delta, 'G1': G1, 'G2': G2, 'norm_w': norm_w}
    _L0_attn_a_in = _L0_attn_a_setup()

    def _L0_attn_b_setup():
        import jax, jax.numpy as jnp
        import numpy as np
        B, L, D = (4, 256, 128)
        H, DK, DV = (4, 32, 32)
        CHUNK = 32
        MIN_FLOOR, MAX_FLOOR = (0.01, 0.1)
        EPS = 1e-05

        def _l2norm(x):
            return x * jax.lax.rsqrt(jnp.sum(x * x, -1, keepdims=True) + 1e-06)

        def _causal_dwconv(x, w):
            b, l, c = x.shape
            k = w.shape[-1]
            xt = jnp.transpose(x, (0, 2, 1))
            y = jax.lax.conv_general_dilated(xt, w[:, None, :], (1,), [(k - 1, 0)], dimension_numbers=('NCH', 'OIH', 'NCH'), feature_group_count=c)
            return jnp.transpose(y, (0, 2, 1))

        def _delta_rule_chunkwise(q, k, v, beta, chunk=CHUNK):
            b, h, l, dk = q.shape
            dv = v.shape[-1]
            q = _l2norm(q)
            k = _l2norm(k)
            v = v * beta[..., None]
            kb = k * beta[..., None]
            n = l // chunk
            resh = lambda t: t.reshape(b, h, n, chunk, t.shape[-1])
            q, k, v, kb = (resh(q), resh(k), resh(v), resh(kb))
            tri = jnp.triu(jnp.ones((chunk, chunk), bool))
            strict = jnp.triu(jnp.ones((chunk, chunk), bool), 1)
            att = jnp.where(tri, 0.0, -(kb @ jnp.swapaxes(k, -1, -2)))
            for i in range(1, chunk):
                upd = jnp.einsum('bhnj,bhnjk->bhnk', att[..., i, :], att)
                att = att.at[..., i, :i].add(upd[..., :i])
            att = att + jnp.eye(chunk, dtype=att.dtype)
            u = att @ v
            w = att @ kb

            def step(S, xs):
                q_i, k_i, u_i, w_i = xs
                local = jnp.where(strict, 0.0, q_i @ jnp.swapaxes(k_i, -1, -2))
                u_adj = u_i - w_i @ S
                o_i = q_i @ S + local @ u_adj
                return (S + jnp.swapaxes(k_i, -1, -2) @ u_adj, o_i)
            xs = tuple((jnp.moveaxis(t, 2, 0) for t in (q, k, u, w)))
            S0 = jnp.zeros((b, h, dk, dv), q.dtype)
            S, o = jax.lax.scan(step, S0, xs)
            return (jnp.moveaxis(o, 0, 2).reshape(b, h, l, dv), S)

        def _rmsnorm(x, w):
            return x * jax.lax.rsqrt(jnp.mean(x * x, -1, keepdims=True) + EPS) * w
        key = jax.random.key(seed)
        ks = jax.random.split(key, 16)
        s = 0.02
        return {'hidden_states': jax.random.normal(ks[0], (B, L, D), jnp.float32), 'W_q': jax.random.normal(ks[1], (D, H * DK), jnp.float32) * s, 'W_k': jax.random.normal(ks[2], (D, H * DK), jnp.float32) * s, 'W_v': jax.random.normal(ks[3], (D, H * DV), jnp.float32) * s, 'W_b': jax.random.normal(ks[4], (D, H), jnp.float32) * s, 'conv_w_q': jax.random.normal(ks[5], (H * DK, 4), jnp.float32) * 0.3, 'conv_w_k': jax.random.normal(ks[6], (H * DK, 4), jnp.float32) * 0.3, 'conv_w_v': jax.random.normal(ks[7], (H * DV, 4), jnp.float32) * 0.3, 'fir_short_w': jax.random.normal(ks[8], (H, DV, 3), jnp.float32) * 0.1, 'fir_long_w': jax.random.normal(ks[9], (H, DV, 31), jnp.float32) * 0.1, 'W_fuse1': jax.random.normal(ks[10], (D + 3 * H * DV, 2 * D), jnp.float32) * s, 'b_fuse1': jnp.zeros((2 * D,), jnp.float32), 'W_fuse2': jax.random.normal(ks[11], (2 * D, H * 4), jnp.float32) * s, 'b_fuse2': jnp.zeros((H * 4,), jnp.float32).at[3::4].set(4.0), 'others_log_tau': jnp.zeros((H,), jnp.float32), 'norm_w': jnp.ones((DV,), jnp.float32), 'W_o': jax.random.normal(ks[12], (H * DV, D), jnp.float32) * s}
    _L0_attn_b_in = _L0_attn_b_setup()

    def _L0_ffn_setup():
        import jax, jax.numpy as jnp
        import numpy as np
        B, S, D, E, H = (2, 128, 128, 16, 256)
        TOP_K = 2
        TEMP = 1.0
        key = jax.random.key(seed)
        ks = jax.random.split(key, 4)
        sc_d = 1.0 / np.sqrt(D)
        sc_h = 1.0 / np.sqrt(H)
        return {'x': jax.random.normal(ks[0], (B, S, D), dtype=jnp.float32), 'Wr': jax.random.normal(ks[1], (D, E), dtype=jnp.float32) * sc_d, 'br': jnp.zeros((E,), dtype=jnp.float32), 'W1': jax.random.normal(ks[2], (E, D, H), dtype=jnp.float32) * sc_d, 'b1': jnp.zeros((E, H), dtype=jnp.float32), 'W2': jax.random.normal(ks[3], (E, H, D), dtype=jnp.float32) * sc_h, 'b2': jnp.zeros((E, D), dtype=jnp.float32)}
    _L0_ffn_in = _L0_ffn_setup()
    _d = {'L0_attn_a_x': _L0_attn_a_in['x'], 'L0_attn_a_Wq': _L0_attn_a_in['Wq'], 'L0_attn_a_Wk': _L0_attn_a_in['Wk'], 'L0_attn_a_Wv': _L0_attn_a_in['Wv'], 'L0_attn_a_Wo': _L0_attn_a_in['Wo'], 'L0_attn_a_delta': _L0_attn_a_in['delta'], 'L0_attn_a_G1': _L0_attn_a_in['G1'], 'L0_attn_a_G2': _L0_attn_a_in['G2'], 'L0_attn_a_norm_w': _L0_attn_a_in['norm_w'], 'L0_attn_b_W_q': _L0_attn_b_in['W_q'], 'L0_attn_b_W_k': _L0_attn_b_in['W_k'], 'L0_attn_b_W_v': _L0_attn_b_in['W_v'], 'L0_attn_b_W_b': _L0_attn_b_in['W_b'], 'L0_attn_b_conv_w_q': _L0_attn_b_in['conv_w_q'], 'L0_attn_b_conv_w_k': _L0_attn_b_in['conv_w_k'], 'L0_attn_b_conv_w_v': _L0_attn_b_in['conv_w_v'], 'L0_attn_b_fir_short_w': _L0_attn_b_in['fir_short_w'], 'L0_attn_b_fir_long_w': _L0_attn_b_in['fir_long_w'], 'L0_attn_b_W_fuse1': _L0_attn_b_in['W_fuse1'], 'L0_attn_b_b_fuse1': _L0_attn_b_in['b_fuse1'], 'L0_attn_b_W_fuse2': _L0_attn_b_in['W_fuse2'], 'L0_attn_b_b_fuse2': _L0_attn_b_in['b_fuse2'], 'L0_attn_b_others_log_tau': _L0_attn_b_in['others_log_tau'], 'L0_attn_b_norm_w': _L0_attn_b_in['norm_w'], 'L0_attn_b_W_o': _L0_attn_b_in['W_o'], 'L0_ffn_Wr': _L0_ffn_in['Wr'], 'L0_ffn_br': _L0_ffn_in['br'], 'L0_ffn_W1': _L0_ffn_in['W1'], 'L0_ffn_b1': _L0_ffn_in['b1'], 'L0_ffn_W2': _L0_ffn_in['W2'], 'L0_ffn_b2': _L0_ffn_in['b2']}
    _x0 = _d['L0_attn_a_x']
    _d['L0_attn_a_x'] = jax.random.normal(jax.random.fold_in(jax.random.key(seed), 1), (1, 2048, 128), dtype=_x0.dtype)
    del _x0
    return _d

def reference(L0_attn_a_x, L0_attn_a_Wq, L0_attn_a_Wk, L0_attn_a_Wv, L0_attn_a_Wo, L0_attn_a_delta, L0_attn_a_G1, L0_attn_a_G2, L0_attn_a_norm_w, L0_attn_b_W_q, L0_attn_b_W_k, L0_attn_b_W_v, L0_attn_b_W_b, L0_attn_b_conv_w_q, L0_attn_b_conv_w_k, L0_attn_b_conv_w_v, L0_attn_b_fir_short_w, L0_attn_b_fir_long_w, L0_attn_b_W_fuse1, L0_attn_b_b_fuse1, L0_attn_b_W_fuse2, L0_attn_b_b_fuse2, L0_attn_b_others_log_tau, L0_attn_b_norm_w, L0_attn_b_W_o, L0_ffn_Wr, L0_ffn_br, L0_ffn_W1, L0_ffn_b1, L0_ffn_W2, L0_ffn_b2):

    def _L0_attn_a_ref(x, Wq, Wk, Wv, Wo, delta, G1, G2, norm_w):
        import jax, jax.numpy as jnp
        import numpy as np
        E = 128
        D = 64
        H = E // D
        EPS = 1e-05
        B, T, _ = x.shape
        q = jax.nn.silu(x @ Wq)
        v = x @ Wv
        log_f = jax.nn.log_sigmoid(x @ Wk + delta)
        k = -jnp.expm1(log_f)

        def to_tbhd(a):
            return a.reshape(B, T, H, D).transpose(1, 0, 2, 3)
        qh, kh, vh, gh = map(to_tbhd, (q, k, v, log_f))
        S0 = jnp.zeros((B, H, D, D), x.dtype)

        def step(S, inp):
            q_t, k_t, v_t, g_t = inp
            S = S * jnp.exp(g_t)[..., None] + k_t[..., None] * v_t[..., None, :]
            o_t = jnp.einsum('bhk,bhkv->bhv', q_t, S)
            return (S, o_t)
        _, o = jax.lax.scan(step, S0, (qh, kh, vh, gh))
        o = o.transpose(1, 0, 2, 3).reshape(B, T, E)
        gate = x @ G1 @ G2
        o = o * jax.nn.sigmoid(gate)
        og = o.reshape(B, T, H, D)
        og = og * jax.lax.rsqrt(jnp.mean(og * og, axis=-1, keepdims=True) + EPS)
        o = og.reshape(B, T, E) * norm_w
        return o @ Wo

    def _L0_attn_b_ref(hidden_states, W_q, W_k, W_v, W_b, conv_w_q, conv_w_k, conv_w_v, fir_short_w, fir_long_w, W_fuse1, b_fuse1, W_fuse2, b_fuse2, others_log_tau, norm_w, W_o):
        import jax, jax.numpy as jnp
        import numpy as np
        B, L, D = (4, 256, 128)
        H, DK, DV = (4, 32, 32)
        CHUNK = 32
        MIN_FLOOR, MAX_FLOOR = (0.01, 0.1)
        EPS = 1e-05

        def _l2norm(x):
            return x * jax.lax.rsqrt(jnp.sum(x * x, -1, keepdims=True) + 1e-06)

        def _causal_dwconv(x, w):
            b, l, c = x.shape
            k = w.shape[-1]
            xt = jnp.transpose(x, (0, 2, 1))
            y = jax.lax.conv_general_dilated(xt, w[:, None, :], (1,), [(k - 1, 0)], dimension_numbers=('NCH', 'OIH', 'NCH'), feature_group_count=c)
            return jnp.transpose(y, (0, 2, 1))

        def _delta_rule_chunkwise(q, k, v, beta, chunk=CHUNK):
            b, h, l, dk = q.shape
            dv = v.shape[-1]
            q = _l2norm(q)
            k = _l2norm(k)
            v = v * beta[..., None]
            kb = k * beta[..., None]
            n = l // chunk
            resh = lambda t: t.reshape(b, h, n, chunk, t.shape[-1])
            q, k, v, kb = (resh(q), resh(k), resh(v), resh(kb))
            tri = jnp.triu(jnp.ones((chunk, chunk), bool))
            strict = jnp.triu(jnp.ones((chunk, chunk), bool), 1)
            att = jnp.where(tri, 0.0, -(kb @ jnp.swapaxes(k, -1, -2)))
            for i in range(1, chunk):
                upd = jnp.einsum('bhnj,bhnjk->bhnk', att[..., i, :], att)
                att = att.at[..., i, :i].add(upd[..., :i])
            att = att + jnp.eye(chunk, dtype=att.dtype)
            u = att @ v
            w = att @ kb

            def step(S, xs):
                q_i, k_i, u_i, w_i = xs
                local = jnp.where(strict, 0.0, q_i @ jnp.swapaxes(k_i, -1, -2))
                u_adj = u_i - w_i @ S
                o_i = q_i @ S + local @ u_adj
                return (S + jnp.swapaxes(k_i, -1, -2) @ u_adj, o_i)
            xs = tuple((jnp.moveaxis(t, 2, 0) for t in (q, k, u, w)))
            S0 = jnp.zeros((b, h, dk, dv), q.dtype)
            S, o = jax.lax.scan(step, S0, xs)
            return (jnp.moveaxis(o, 0, 2).reshape(b, h, l, dv), S)

        def _rmsnorm(x, w):
            return x * jax.lax.rsqrt(jnp.mean(x * x, -1, keepdims=True) + EPS) * w
        b, l, d = hidden_states.shape
        q = jax.nn.silu(_causal_dwconv(hidden_states @ W_q, conv_w_q))
        k = jax.nn.silu(_causal_dwconv(hidden_states @ W_k, conv_w_k))
        v = jax.nn.silu(_causal_dwconv(hidden_states @ W_v, conv_w_v))
        q = q.reshape(b, l, H, DK)
        k = k.reshape(b, l, H, DK)
        v = v.reshape(b, l, H, DV)
        beta = jax.nn.sigmoid(hidden_states @ W_b)
        delta_out, _ = _delta_rule_chunkwise(jnp.transpose(q, (0, 2, 1, 3)), jnp.transpose(k, (0, 2, 1, 3)), jnp.transpose(v, (0, 2, 1, 3)), jnp.transpose(beta, (0, 2, 1)))
        delta_out = jnp.transpose(delta_out, (0, 2, 1, 3))
        vc = v.reshape(b, l, H * DV)
        fir_s = _causal_dwconv(vc, fir_short_w.reshape(H * DV, -1)).reshape(b, l, H, DV)
        fir_l = _causal_dwconv(vc, fir_long_w.reshape(H * DV, -1)).reshape(b, l, H, DV)
        gate_in = jnp.concatenate([hidden_states, fir_s.reshape(b, l, -1), fir_l.reshape(b, l, -1), delta_out.reshape(b, l, -1)], -1)
        hid = jax.nn.gelu(gate_in @ W_fuse1 + b_fuse1, approximate=False)
        logits = (hid @ W_fuse2 + b_fuse2).reshape(b, l, H, 4)
        p_raw = jax.nn.sigmoid(logits[..., 3])
        floor = MIN_FLOOR + (MAX_FLOOR - MIN_FLOOR) * (1.0 - p_raw)
        p_val = (1.0 - floor) * p_raw
        tau = jnp.exp(others_log_tau)
        others = jax.nn.softmax(logits[..., :3] / tau[None, None, :, None], -1)
        p_ctx = (1.0 - p_val)[..., None] * others
        o = p_ctx[..., 0:1] * fir_s + p_ctx[..., 1:2] * fir_l + p_ctx[..., 2:3] * delta_out + p_val[..., None] * v
        o = _rmsnorm(o, norm_w)
        return o.reshape(b, l, H * DV) @ W_o

    def _L0_ffn_ref(x, Wr, br, W1, b1, W2, b2):
        import jax, jax.numpy as jnp
        import numpy as np
        B, S, D, E, H = (2, 128, 128, 16, 256)
        TOP_K = 2
        TEMP = 1.0
        token_shape = x.shape[:-1]
        d = x.shape[-1]
        xt = x.reshape(-1, d)
        T = xt.shape[0]
        logits = (xt @ Wr + br) / TEMP
        probs = jax.nn.softmax(logits, axis=-1)
        w, idx = jax.lax.top_k(probs, TOP_K)
        w = w / jnp.clip(jnp.sum(w, axis=-1, keepdims=True), 1e-09)
        comb = jnp.zeros((T, E), dtype=xt.dtype)
        comb = comb.at[jnp.arange(T)[:, None], idx].add(w)
        h = jax.nn.gelu(jnp.einsum('td,edh->teh', xt, W1) + b1, approximate=False)
        o = jnp.einsum('teh,eho->teo', h, W2) + b2
        y = jnp.einsum('teo,te->to', o, comb)
        y = xt + y
        return y.reshape(*token_shape, d)
    x = L0_attn_a_x
    x = x + _L0_attn_a_ref(_layernorm(x, axis=-1), L0_attn_a_Wq, L0_attn_a_Wk, L0_attn_a_Wv, L0_attn_a_Wo, L0_attn_a_delta, L0_attn_a_G1, L0_attn_a_G2, L0_attn_a_norm_w)
    x = x + _L0_ffn_ref(_layernorm(x, axis=-1), L0_ffn_Wr, L0_ffn_br, L0_ffn_W1, L0_ffn_b1, L0_ffn_W2, L0_ffn_b2)
    x = x + _L0_attn_b_ref(_layernorm(x, axis=-1), L0_attn_b_W_q, L0_attn_b_W_k, L0_attn_b_W_v, L0_attn_b_W_b, L0_attn_b_conv_w_q, L0_attn_b_conv_w_k, L0_attn_b_conv_w_v, L0_attn_b_fir_short_w, L0_attn_b_fir_long_w, L0_attn_b_W_fuse1, L0_attn_b_b_fuse1, L0_attn_b_W_fuse2, L0_attn_b_b_fuse2, L0_attn_b_others_log_tau, L0_attn_b_norm_w, L0_attn_b_W_o)
    x = x + _L0_ffn_ref(_layernorm(x, axis=-1), L0_ffn_Wr, L0_ffn_br, L0_ffn_W1, L0_ffn_b1, L0_ffn_W2, L0_ffn_b2)
    return x

_drawn_inputs = setup_inputs


def setup_inputs(seed=0):
    import zlib

    import numpy as np

    out = dict(_drawn_inputs(seed))
    spreads = {'L0_attn_a_delta': (4.595119953155518, 0.2),
     'L0_attn_a_norm_w': (1.0, 0.2),
     'L0_attn_b_b_fuse1': (0.0, 0.8),
     'L0_attn_b_others_log_tau': (0.0, 0.8),
     'L0_attn_b_norm_w': (1.0, 0.538),
     'L0_ffn_br': (0.0, 0.1),
     'L0_ffn_b1': (0.0, 0.1),
     'L0_ffn_b2': (0.0, 0.1)}
    factors = {'L0_attn_a_G1': 3.535,
     'L0_attn_a_G2': 3.897,
     'L0_attn_b_W_q': 69.762,
     'L0_attn_b_W_k': 21.898,
     'L0_attn_b_W_b': 99.25,
     'L0_attn_b_conv_w_q': 69.545,
     'L0_attn_b_conv_w_k': 22.636,
     'L0_attn_b_fir_short_w': 8.0,
     'L0_attn_b_fir_long_w': 8.0,
     'L0_attn_b_W_fuse1': 8.0,
     'L0_attn_b_W_fuse2': 8.0}
    for name, (base, spread) in spreads.items():
        noise = np.random.default_rng([zlib.crc32(name.encode()), seed]).standard_normal(out[name].shape)
        drawn = base * np.exp(spread * noise) if base else spread * noise
        out[name] = jnp.asarray(drawn.astype(out[name].dtype))
    for name, factor in factors.items():
        out[name] = (out[name] * factor).astype(out[name].dtype)
    return out
```

```python
from contextlib import ExitStack

import concourse.bass as bass
from concourse import mybir

ALU = mybir.AluOpType
ACT = mybir.ActivationFunctionType
AX = mybir.AxisListType.X
F32 = mybir.dt.float32
BF16 = mybir.dt.bfloat16
I32 = mybir.dt.int32
U32 = mybir.dt.uint32

P = 128
NT = 4
N = NT * P
CH = 32
NC = N // CH
LN_EPS = 1e-5
MAX_DECAY = 20.0
Z_MIN = -40.0
EXP_MIN = -80.0


def hybrid_kernel(nc, x, wq, wk, wv, wo, delta, g1, g2, norm_w, bwq, bwk, bwv, bwb, cwq, cwk, cwv, fir_s, fir_l,
                  wf1, bf1, wf2, bf2, log_tau, bnorm_w, bwo, wr, br, w1, b1, w2, b2, out):
    T = x.shape[1]
    NB = T // N
    E, _, HID = w1.shape
    HH = HID // P
    AH, AD = 2, 64
    BH, BD = 4, 32
    CAT = 3 * P
    TAPS = cwq.shape[1]
    HALO = TAPS - 1
    FS, FL = fir_s.shape[2], fir_l.shape[2]
    VHALO = FL - 1
    G = BH * NT

    ctx = ExitStack()
    with ctx:
        def sb(name, shape, dt=F32):
            return ctx.enter_context(nc.sbuf_tensor(name, shape, dt))

        def sem(name):
            return ctx.enter_context(nc.semaphore(name))

        turn_sems = []

        def bsem(name):
            s = sem(name)
            turn_sems.append(s)
            return s

        bank = [ctx.enter_context(nc.psum_tensor(f"bank{i}", [P, 512], F32)) for i in range(8)]
        B0, B1, B2, B3, B4, B5, B6, STATE = bank

        X = sb("X", [P, T // P, P])
        Wq, Wk, Wv, Wo = (sb(n, [P, P]) for n in ("Wq", "Wk", "Wv", "Wo"))
        G1 = sb("G1", [P, AD])
        G2 = sb("G2", [AD, P])
        bWo, bWb = sb("bWo", [P, P]), sb("bWb", [P, BH])
        Wraw = sb("Wraw", [P, 3, P])
        WrawT = sb("WrawT", [P, 3, P])
        Wtap = sb("Wtap", [P, 3, P])
        WC = sb("WC", [P, TAPS, CAT])
        cw = sb("cw", [P, 3, TAPS])
        firs, firl = sb("firs", [P, FS]), sb("firl", [P, FL])
        Wf1 = sb("Wf1", [P, 4, HID])
        Wf2 = sb("Wf2", [P, HH, 4 * BH])
        bf1c = sb("bf1c", [P, HH])
        W1h, W1l = sb("W1h", [P, E, HID], BF16), sb("W1l", [P, E, HID], BF16)
        W2 = sb("W2", [P, E, HH, P])
        Wr = sb("Wr", [P, E])
        b1rows = sb("b1rows", [E * HH, P])
        b1c = sb("b1c", [P, E * HH])
        b2r = sb("b2r", [E, P])
        brow, bf2row = sb("brow", [1, E]), sb("bf2row", [1, 4 * BH])
        deltac, normc, bnormc = sb("deltac", [P, 1]), sb("normc", [P, 1]), sb("bnormc", [P, 1])
        itau = sb("itau", [P, BH])
        ident = sb("ident", [P, P])
        ones = sb("ones", [1, P])
        mhalf = sb("mhalf", [P, 512])
        iota_e = sb("iota_e", [P, E])
        scan_on = sb("scan_on", [P, N])
        m8 = sb("m8", [P, NT, P])
        m16 = sb("m16", [P, NT * 8, 8])
        m32 = sb("m32", [P, NT * 4, 16])
        upneg, upinc = sb("upneg", [P, NT, P]), sb("upinc", [P, NT, P])
        same = sb("same", [P, P])
        lev = sb("lev", [P, 5, BD])
        idc = sb("idc", [P, BD])
        zeros = sb("zeros", [P, P])
        st, mv = sb("st", [P, NT, 6]), sb("mv", [P, NT, 2])
        var, rstd = sb("var", [P, NT]), sb("rstd", [P, NT])
        xn = sb("xn", [P, NT, P])
        xT = sb("xT", [P, HALO + N])
        scratch = sb("scratch", [P, 19 * 1024])
        used = [0]

        def cut(shape):
            n = 1
            for d in shape[1:]:
                n *= d
            v = scratch[:, used[0]:used[0] + n]
            used[0] += n
            names = "abc"[:len(shape) - 1]
            if len(names) > 1:
                v = v.rearrange(f"p ({' '.join(names)}) -> p {' '.join(names)}",
                                **{k: d for k, d in zip(names[1:], shape[2:])})
            return v

        z, ez, rz, qc, eq, rq = (cut([P, N]) for _ in range(6))
        qs, ks, lnf, H = (cut([P, N]) for _ in range(4))
        D8, D16, D32, DT = (cut([P, N]) for _ in range(4))
        E8q, E8k, E16, E32, Ei, Et = (cut([P, N]) for _ in range(6))
        q8, k8, qk16, qk32, qi, ki = (cut([P, N]) for _ in range(6))
        Fd = sb("Fd", [P, NC])
        g1T = sb("g1T", [AD, N])
        sg = cut([P, NT, P])
        va = cut([P, NT, P])
        kt = cut([P, NT, P])
        AT = sb("AT", [P, AH, NT, P])
        SA = sb("SA", [P, NC + 1, AD])
        og, osq = sb("og", [P, NT, P]), sb("osq", [P, NT, P])
        ss, ssr = sb("ss", [P, 32]), sb("ssr", [P, 32])
        oT = sb("oT", [P, N])
        xh, xl = sb("xh", [P, N], BF16), sb("xl", [P, N], BF16)
        acc = sb("acc", [P, NT, P])
        lg = sb("lg", [P, NT, E])
        top = sb("top", [P, NT, 8])
        topi = sb("topi", [P, NT, 8], U32)
        topf = sb("topf", [P, NT, 8])
        gap, th, wa, wb = (sb(n, [P, NT]) for n in ("gap", "th", "wa", "wb"))
        comb, comb2 = sb("comb", [P, NT, E]), sb("comb2", [P, NT, E])
        cT = sb("cT", [E, N])
        h = sb("h", [P, 2, HH, N])
        W1f = h[:, :, :, :].rearrange("p a m n -> p (a m n)").rearrange("p (e n) -> p e n", n=HID)
        EH = E // 2
        used[0] = 0
        QB = CAT + BH
        thB = cut([P, NT, QB])
        s2 = cut([P, NT, CAT])
        s2q = cut([P, NT, 2 * P])
        qn, kn, kb, vB = (cut([P, NT, P]) for _ in range(4))
        beta = cut([P, NT, BH])
        VK = cut([P, NT, BH, 2 * BD])
        qT, knT, kbT = (cut([P, N]) for _ in range(3))
        vT = sb("vT", [P, VHALO + N])
        fs, flA, flB = (cut([P, N]) for _ in range(3))
        BA = cut([P, BH, NT, P])
        LT = cut([P, BH, NT, P])
        Tc, TTc, Yc = (cut([P, G, BD]) for _ in range(3))
        BDT = sb("BDT", [P, G, P])
        U, Wt = cut([P, NT, P]), cut([P, NT, P])
        wT = cut([P, N])
        ua = cut([P, NT, P])
        Sbd = sb("Sbd", [P, P])
        dl = cut([P, NT, P])
        dT = cut([P, N])
        hid = LT[:, 0:HH, :, :].rearrange("p m t i -> p m (t i)")
        l2 = cut([P, NT, BH, 4])
        t3, pr, pv, ls, lsm = (cut(s) for s in ([P, NT, BH], [P, NT, BH], [P, NT, BH], [P, NT, BH, 3], [P, NT, BH]))
        pe_, rs_, cc = cut([P, NT, BH, 3]), cut([P, NT, BH]), cut([P, NT, BH])
        pc = cut([P, NT, BH, 3])
        m1_, m2_, m3_, m4_ = (BA[:, i, :, :] for i in range(4))

        assert used[0] <= scratch.shape[1]

        l_x, l_a, l_b, l_small, l_w1, l_w2 = (sem(n) for n in ("l_x", "l_a", "l_b", "l_small", "l_w1", "l_w2"))
        const_steps, consts, w1_split = sem("const_steps"), sem("consts"), sem("w1_split")
        s_rawT, s_rawTs, s_tap, s_tapT, s_tapS, s_b1T, s_itau = (
            sem(n) for n in ("s_rawT", "s_rawTs", "s_tap", "s_tapT", "s_tapS", "s_b1T", "s_itau"))
        zeroed, s_state0 = sem("zeroed"), sem("s_state0")
        lev_built, lev_copied = sem("lev_built"), sem("lev_copied")
        stored, arrive, go = sem("stored"), sem("arrive"), sem("go")

        vstep, astep, gstep = bsem("vector_steps"), bsem("scalar_steps"), bsem("gpsimd_steps")
        ln_var, ln_rstd, ln_xn, ln_xT, ln_xTs, xl_ready, x_ready = (
            bsem(n) for n in ("ln_var", "ln_rstd", "ln_xn", "ln_xT", "ln_xTs", "xl_ready", "x_ready"))
        a_proj, a_gate, a_g1s, a_vs, a_z, a_qc, a_ez, a_eq, a_ez1, a_lnf, a_gz = (
            bsem(n) for n in ("a_proj", "a_gate", "a_g1s", "a_vs", "a_z", "a_qc", "a_ez", "a_eq", "a_ez1", "a_lnf", "a_gz"))
        a_eg, a_H, a_DT, a_D8, a_D16, a_D32, a_exps, a_qk, a_qkv, a_k, a_ki = (
            bsem(n) for n in ("a_eg", "a_H", "a_DT", "a_D8", "a_D16", "a_D32", "a_exps", "a_qk", "a_qkv", "a_k", "a_ki"))
        a_sc, a_AT, a_kiT, a_kts, a_KV, a_S, a_o, a_og, a_osq, rms_var, rms_r, a_on, a_oT, a_oTs, a_out = (
            bsem(n) for n in ("a_sc", "a_AT", "a_kiT", "a_kts", "a_KV", "a_S", "a_o", "a_og", "a_osq", "rms_var", "rms_r",
                              "a_on", "a_oT", "a_oTs", "a_out"))
        f_lg, f_gap, f_th, f_comb, f_cT, f_cTs, f_b2, f_up, f_h, f_dn, f_acc = (
            bsem(n) for n in ("f_lg", "f_gap", "f_th", "f_comb", "f_cT", "f_cTs", "f_b2", "f_up", "f_h", "f_dn", "f_acc"))
        b_conv, b_th, b_s2, b_sq, b_ss, b_rn, b_q, b_kn, b_kb, b_v, b_vk, b_halo = (
            bsem(n) for n in ("b_conv", "b_th", "b_s2", "b_sq", "b_ss", "b_rn", "b_q", "b_kn", "b_kb", "b_v", "b_vk", "b_halo"))
        b_tr, b_trs, b_vTs, b_knk, b_BA, b_loc, b_LT, b_Y, b_Ys, b_Z, b_T, b_bd, b_UW, b_UWs, b_wT, b_wTs = (
            bsem(n) for n in ("b_tr", "b_trs", "b_vTs", "b_knk", "b_BA", "b_loc", "b_LT", "b_Y", "b_Ys", "b_Z", "b_T", "b_bd",
                              "b_UW", "b_UWs", "b_wT", "b_wTs"))
        c_wS, c_ua, c_acc, c_S, c_o, b_fs, b_fl, b_dTs, b_dls, b_dT, b_hid, b_hids, b_lg, b_l3, b_t3, b_lsm, b_pe, b_ft = (
            bsem(n) for n in ("c_wS", "c_ua", "c_acc", "c_S", "c_o", "b_fs", "b_fl", "b_dTs", "b_dls", "b_dT", "b_hid",
                              "b_hids", "b_lg", "b_l3", "b_t3", "b_lsm", "b_pe", "b_ft"))
        b_mix, b_osq, b_on, b_oT, b_oTs, b_out = (bsem(n) for n in ("b_mix", "b_osq", "b_on", "b_oT", "b_oTs", "b_out"))

        def flat(t):
            return t[:, :, :].rearrange("p t d -> p (t d)")

        def tile(t, i):
            return t[:, i * P:(i + 1) * P]

        def heads(t):
            return t[:, :, :].rearrange("p t (h d) -> p (t h) d", d=BD)

        def spread(ap, n):
            return ap.unsqueeze(2).broadcast_to([P, ap.shape[1], n])

        x_dram = x[0].rearrange("(t p) d -> p t d", p=P)
        out_dram = out[0].rearrange("(t p) d -> p t d", p=P)

        def turn_over(eng, b):
            eng.drain().then_inc(arrive, 1)
            eng.wait_ge(go, b + 1)

        block = ctx.enter_context(nc.Block())

        @block.sync
        def _(sp):
            sp.dma_start(X[:, :, :], x_dram).then_inc(l_x, 16)
            for t, src in ((Wq, wq), (Wk, wk), (Wv, wv), (Wo, wo), (G1, g1), (G2, g2)):
                sp.dma_start(t[:, :], src).then_inc(l_a, 16)
            col = "(p a) -> p a"
            sp.dma_start(deltac[:, :], delta.rearrange(col, a=1)).then_inc(l_a, 16)
            sp.dma_start(normc[:, :], norm_w.rearrange(col, a=1)).then_inc(l_a, 16)
            for i, (w, c) in enumerate(((bwq, cwq), (bwk, cwk), (bwv, cwv))):
                sp.dma_start(Wraw[:, i, :], w).then_inc(l_b, 16)
                sp.dma_start(cw[:, i, :], c).then_inc(l_b, 16)
            sp.dma_start(Wr[:, :], wr).then_inc(l_small, 16)
            sp.dma_start(brow[:, :], br.rearrange("(a n) -> a n", a=1)).then_inc(l_small, 16)
            sp.dma_start(b1rows[:, :], b1.rearrange("e (m h) -> (e m) h", h=P)).then_inc(l_small, 16)
            sp.dma_start(b2r[:, :], b2).then_inc(l_small, 16)
            sp.dma_start(bWb[:, :], bwb).then_inc(l_small, 16)
            sp.dma_start(bWo[:, :], bwo).then_inc(l_small, 16)
            sp.dma_start(firs[:, :], fir_s.rearrange("h d k -> (h d) k")).then_inc(l_small, 16)
            sp.dma_start(firl[:, :], fir_l.rearrange("h d k -> (h d) k")).then_inc(l_small, 16)
            sp.dma_start(Wf1[:, :, :], wf1.rearrange("(k p) n -> p k n", p=P)).then_inc(l_small, 16)
            sp.dma_start(Wf2[:, :, :], wf2.rearrange("(k p) n -> p k n", p=P)).then_inc(l_small, 16)
            for m in range(HH):
                sp.dma_start(bf1c[:, m:m + 1], bf1[m * P:(m + 1) * P].rearrange(col, a=1)).then_inc(l_small, 16)
            sp.dma_start(bf2row[:, :], bf2.rearrange("(a n) -> a n", a=1)).then_inc(l_small, 16)
            for i in range(BH):
                sp.dma_start(bnormc[i * BD:(i + 1) * BD, :], bnorm_w.rearrange(col, a=1)).then_inc(l_small, 16)
            sp.dma_start(itau[:, :], log_tau.rearrange("(a n) -> a n", a=1).broadcast_to([P, BH])).then_inc(l_small, 16)
            for i in range(2):
                if i:
                    sp.wait_ge(w1_split, i)
                sp.dma_start(W1f[:, :, :], w1[i * EH:(i + 1) * EH].rearrange("e d h -> d e h")).then_inc(l_w1, 16)
            with sp.Fori(0, NB) as b:
                sp.wait_ge(x_ready, 4)
                sp.dma_start(out_dram[:, bass.ds(b * NT, NT), :], X[:, bass.ds(b * NT, NT), :]).then_inc(stored, 16)
                sp.wait_ge(arrive, 4)
                for s in turn_sems + [arrive]:
                    sp.sem_clear(s)
                sp.sem_inc(go, 1)
            sp.wait_ge(stored, 16 * NB)

        N_SMALL = 10 + HH + 1 + BH + 1

        @block.gpsimd
        def _(pool):
            steps = [0]

            def done(ins):
                steps[0] += 1
                ins.then_inc(const_steps, 1)
                pool.wait_ge(const_steps, steps[0])

            def keep(t, pattern, base, cm, fill=0.0, op=ALU.is_ge):
                done(pool.affine_select(out=t, in_=t, compare_op=op, fill=fill, base=base, pattern=pattern,
                                        channel_multiplier=cm))

            done(pool.memset(mhalf[:, :], -0.5))
            done(pool.memset(ones[:, :], 1.0))
            done(pool.memset(zeros[:, :], 0.0))
            done(pool.memset(ident[:, :], 0.0))
            keep(ident[:, :], [[-1, P]], 0, 1, 1.0, ALU.not_equal)
            done(pool.iota(iota_e[:, :].bitcast(I32), pattern=[[1, E]], base=0, channel_multiplier=0))
            done(pool.tensor_copy(iota_e[:, :], iota_e[:, :].bitcast(I32)))
            done(pool.memset(scan_on[:, :], 1.0))
            done(pool.memset(scan_on[:, :].rearrange("p (c i) -> p c i", i=CH)[:, :, 0:1], 0.0))
            done(pool.memset(m8[:, :, :], 1.0))
            keep(m8[:, :, :], [[0, NT], [1, P]], 0, -1)
            keep(m8[:, :, :], [[0, NT], [-8, 16], [0, 8]], 0, 1)
            for m, w in ((m16, 16), (m32, 32)):
                done(pool.memset(m[:, :, :], 1.0))
                k = P // w
                keep(m[:, :, :], [[0, NT], [-w, k], [0, w // 2]], 0, 1)
                keep(m[:, :, :], [[0, NT], [w, k], [0, w // 2]], w // 2 - 1, -1)
            for m, v, s in ((upneg, -1.0, -1), (upinc, 1.0, 0)):
                done(pool.memset(m[:, :, :], v))
                keep(m[:, :, :], [[0, NT], [1, P]], s, -1)
                keep(m[:, :, :], [[0, NT], [-CH, P // CH], [0, CH]], 0, 1)
            done(pool.memset(same[:, :], 1.0))
            keep(same[:, :], [[-CH, P // CH], [0, CH]], 0, 1)
            keep(same[:, :], [[CH, P // CH], [0, CH]], CH - 1, -1)
            done(pool.memset(lev[:, :, :], 0.0))
            done(pool.memset(idc[:, :], 0.0))
            for l in range(5):
                w = 2 << l
                left = lev[0:CH, l, :].rearrange("p (k i) -> p k i", i=w)[:, :, 0:w // 2]
                done(pool.memset(left, 1.0))
                keep(left, [[-w, CH // w], [0, w // 2]], -(w // 2), 1)
                keep(left, [[w, CH // w], [0, w // 2]], w - 1, -1)
            for c in range(P // CH):
                keep(idc[c * CH:(c + 1) * CH, :], [[-1, CH]], 0, 1, 1.0, ALU.not_equal)
                if c:
                    done(pool.tensor_copy(lev[c * CH:(c + 1) * CH, :, :], lev[0:CH, :, :]))
            pool.nop().then_inc(consts, 1)
            for i in range(2):
                half = slice(i * EH, (i + 1) * EH)
                pool.wait_ge(l_w1, 16 * (i + 1))
                done(pool.tensor_copy(W1h[:, half, :], W1f[:, :, :]))
                pool.tensor_tensor(W1l[:, half, :], W1f[:, :, :], W1h[:, half, :], ALU.subtract).then_inc(w1_split, 1)

            def power(out_, in_, n, waits, value, done_sem):
                pool.wait_ge(waits, value)
                pool.tensor_tensor(out_, in_, mhalf[:, 0:n], ALU.pow).then_inc(done_sem, 1)

            with pool.Fori(0, NB) as b:
                power(rstd[:, :], var[:, :], NT, ln_var, 1, ln_rstd)
                pool.wait_ge(a_k, 1)
                pool.wait_ge(a_exps, 6)
                pool.tensor_tensor(ki[:, :], ks[:, :], Et[:, :], ALU.mult).then_inc(a_ki, 1)
                pool.tensor_tensor(qi[:, :], qs[:, :], Ei[:, :], ALU.mult).then_inc(a_ki, 1)
                power(ssr[:, 0:8], ss[:, 0:8], 8, rms_var, 1, rms_r)
                power(rstd[:, :], var[:, :], NT, ln_var, 2, ln_rstd)
                power(rstd[:, :], var[:, :], NT, ln_var, 3, ln_rstd)
                power(ssr[:, 0:32], ss[:, 0:32], 32, b_ss, 1, b_rn)
                power(ssr[:, 0:16], ss[:, 0:16], 16, rms_var, 2, rms_r)
                power(rstd[:, :], var[:, :], NT, ln_var, 4, ln_rstd)
                turn_over(pool, b)

        @block.scalar
        def _(act):
            for e0 in range(0, E, 4):
                act.dma_start(W2[:, e0:e0 + 4, :, :].rearrange("p e m n -> p (e m) n"),
                              w2[e0:e0 + 4].rearrange("e (m p) n -> p (e m) n", p=P)).then_inc(l_w2, 16)
            act.wait_ge(l_small, 16 * N_SMALL)
            act.activation(itau[:, :], itau[:, :], ACT.Exp, scale=-1.0).then_inc(s_itau, 1)
            act.wait_ge(s_rawT, 1)
            act.copy(WrawT[:, :, :].rearrange("p i d -> p (i d)"), B1[:, 0:3 * P]).then_inc(s_rawTs, 1)
            act.wait_ge(s_b1T, 1)
            act.copy(b1c[:, :], B3[:, 0:E * HH]).then_inc(s_rawTs, 1)
            for i in range(TAPS):
                act.wait_ge(s_tapT, i + 1)
                act.copy(WC[:, i, :], B2[:, 0:CAT]).then_inc(s_tapS, 1)

            def evac_xT(u):
                act.wait_ge(ln_xT, u + 1)
                act.copy(xT[:, HALO:HALO + N], B0[:, :]).then_inc(ln_xTs, 1)

            def experts(u):
                for e in range(E):
                    k = u * E + e
                    for m in range(HH):
                        act.wait_ge(f_up, HH * k + m + 1)
                        if e >= 2 and m == 0:
                            act.wait_ge(f_dn, k - 1)
                        act.activation(h[:, e % 2, m, :], bank[3 + 2 * (e % 2) + m][:, :], ACT.Gelu,
                                       bias=b1c[:, e * HH + m:e * HH + m + 1]).then_inc(f_h, 1)

            def moe(u, norm):
                evac_xT(norm)
                act.copy(xh[:, :], B0[:, :]).then_inc(ln_xTs, 1)
                act.wait_ge(f_gap, u + 1)
                act.activation(th[:, :], gap[:, :], ACT.Tanh, scale=0.5).then_inc(f_th, 1)
                act.wait_ge(f_cT, u + 1)
                act.copy(cT[:, :], B2[0:E, :]).then_inc(f_cTs, 1)
                experts(u)

            with act.Fori(0, NB) as b:
                evac_xT(0)
                act.wait_ge(a_z, 1)
                act.activation(ez[:, :], z[:, :], ACT.Exp, scale=-1.0).then_inc(a_ez, 1)
                act.wait_ge(a_proj, 3)
                act.copy(g1T[:, :], B3[0:AD, :]).then_inc(a_g1s, 1)
                act.wait_ge(a_qc, 1)
                act.activation(eq[:, :], qc[:, :], ACT.Exp, scale=-1.0).then_inc(a_eq, 1)
                act.wait_ge(a_ez1, 1)
                act.activation(lnf[:, :], ez[:, :], ACT.Ln).then_inc(a_lnf, 1)
                act.wait_ge(a_proj, 4)
                act.copy(flat(va), B4[:, :]).then_inc(a_vs, 1)
                act.wait_ge(a_H, 1)
                act.activation(Ei[:, :], H[:, :], ACT.Exp, scale=-1.0).then_inc(a_exps, 1)
                act.activation(Fd[:, :], H[:, CH - 1:N:CH], ACT.Exp, scale=-1.0).then_inc(a_exps, 1)
                act.wait_ge(a_D8, 1)
                act.activation(E8q[:, :], D8[:, :], ACT.Exp, scale=-1.0).then_inc(a_exps, 1)
                act.activation(E8k[:, :], D8[:, :], ACT.Exp).then_inc(a_exps, 1)
                act.wait_ge(a_D16, 2)
                act.activation(E16[:, :], D16[:, :], ACT.Exp, scale=-1.0).then_inc(a_exps, 1)
                act.wait_ge(a_DT, 1)
                act.activation(Et[:, :], DT[:, :], ACT.Exp, scale=-1.0).then_inc(a_exps, 1)
                act.wait_ge(a_D32, 2)
                act.activation(E32[:, :], D32[:, :], ACT.Exp, scale=-1.0).then_inc(a_exps, 1)
                act.wait_ge(a_gz, 1)
                act.activation(flat(sg), flat(sg), ACT.Exp, scale=-1.0).then_inc(a_eg, 1)
                act.wait_ge(a_kiT, 1)
                act.copy(flat(kt), B0[:, :]).then_inc(a_kts, 1)
                act.wait_ge(a_og, 1)
                act.activation(flat(osq), flat(og), ACT.Square).then_inc(a_osq, 1)
                act.wait_ge(a_oT, 1)
                act.activation(oT[:, :], B4[:, :], ACT.Copy, scale=normc[:, :]).then_inc(a_oTs, 1)
                moe(0, 1)
                evac_xT(2)
                for t in range(NT):
                    act.wait_ge(b_conv, t + 1)
                    act.activation(thB[:, t, :], bank[1 + t][:, 0:QB], ACT.Tanh, scale=0.5).then_inc(b_th, 1)
                act.wait_ge(b_conv, NT)
                act.copy(xT[:, 0:HALO], xT[:, N:N + HALO]).then_inc(b_halo, 1)
                act.wait_ge(b_s2, NT)
                act.activation(s2q[:, :, :], s2[:, :, 0:2 * P], ACT.Square).then_inc(b_sq, 1)
                act.activation(vB[:, :, :], s2[:, :, 2 * P:CAT], ACT.Copy, scale=0.5).then_inc(b_v, 1)
                act.wait_ge(b_tr, 1)
                act.copy(vT[:, VHALO:VHALO + N], B0[:, :]).then_inc(b_trs, 1)
                act.wait_ge(b_tr, 2)
                act.copy(knT[:, :], B5[:, :]).then_inc(b_trs, 1)
                act.wait_ge(b_tr, 3)
                act.copy(kbT[:, :], B6[:, :]).then_inc(b_trs, 1)
                act.wait_ge(b_tr, 4)
                act.copy(qT[:, :], B1[:, :]).then_inc(b_trs, 1)
                for l in range(5):
                    if l:
                        act.wait_ge(b_Y, l + 1)
                        act.copy(Yc[:, :, :].rearrange("p g i -> p (g i)"), B3[:, :]).then_inc(b_Ys, 1)
                    act.wait_ge(b_T, l + 1)
                    for c in range(2):
                        act.copy(BDT[c * CH:(c + 1) * CH, :, c * CH:(c + 1) * CH],
                                 TTc[c * CH:(c + 1) * CH, :, :]).then_inc(b_bd, 1)
                for i, bk in enumerate((B5, B6)):
                    act.wait_ge(b_UW, i + 1)
                    uw = bk[:, :].rearrange("p (g c) -> p g c", c=2 * BD)
                    for j, d in enumerate((Wt, U)):
                        dst = heads(d)[:, 2 * BH * i:2 * BH * (i + 1), :]
                        act.copy(dst, uw[:, :, BD * (1 - j):BD * (2 - j)]).then_inc(b_UWs, 1)
                act.wait_ge(b_wT, 1)
                act.copy(wT[:, :], B0[:, :]).then_inc(b_wTs, 1)
                act.wait_ge(c_o, NT)
                act.copy(flat(dl), B2[:, :]).then_inc(b_dls, 1)
                act.wait_ge(b_dT, 1)
                act.copy(dT[:, :], B5[:, :]).then_inc(b_dTs, 1)
                for m, bk in enumerate((B6, B0)):
                    act.wait_ge(b_hid, m + 1)
                    act.activation(hid[:, m, :], bk[:, :], ACT.Gelu, bias=bf1c[:, m:m + 1]).then_inc(b_hids, 1)
                act.wait_ge(b_l3, 1)
                act.activation(t3[:, :, :], l2[:, :, :, 3], ACT.Tanh, scale=0.5).then_inc(b_t3, 1)
                act.wait_ge(b_lsm, 1)
                act.activation(pe_[:, :, :, :], ls[:, :, :, :], ACT.Exp).then_inc(b_pe, 1)
                act.wait_ge(b_fl, 1)
                act.copy(vT[:, 0:VHALO], vT[:, N:N + VHALO]).then_inc(b_halo, 1)
                act.wait_ge(b_mix, 1)
                act.activation(flat(osq), flat(og), ACT.Square).then_inc(b_osq, 1)
                act.wait_ge(b_oT, 1)
                act.activation(oT[:, :], B5[:, :], ACT.Copy, scale=bnormc[:, :]).then_inc(b_oTs, 1)
                moe(1, 3)
                turn_over(act, b)

        @block.tensor
        def _(pe):
            pe.wait_ge(consts, 1)
            pe.wait_ge(l_b, 16 * 6)
            for i in range(3):
                mm = pe.transpose(tile(B1, i), Wraw[:, i, :], ident[:, :])
            mm.then_inc(s_rawT, 1)
            pe.wait_ge(l_small, 16 * N_SMALL)
            pe.transpose(B3[:, 0:E * HH], b1rows[:, :], ident[0:E * HH, 0:E * HH]).then_inc(s_b1T, 1)
            for i in range(TAPS):
                pe.wait_ge(s_tap, i + 1)
                if i:
                    pe.wait_ge(s_tapS, i)
                for j in range(3):
                    mm = pe.transpose(tile(B2, j), Wtap[:, j, :], ident[:, :])
                mm.then_inc(s_tapT, 1)
            pe.matmul(STATE[:, 0:P], zeros[:, :], zeros[:, :], start=True, stop=False,
                      skip_group_check=True).then_inc(s_state0, 1)
            pe.wait_ge(l_a, 16 * 8)
            pe.wait_ge(s_tapS, TAPS)
            pe.wait_ge(s_rawTs, 2)
            pe.wait_ge(zeroed, 1)

            def turn_tiles(dst, src, sig):
                for t in range(NT):
                    mm = pe.transpose(tile(dst, t), src[:, t, :], ident[:, :])
                mm.then_inc(sig, 1)

            def norm_T(u):
                pe.wait_ge(ln_xn, u + 1)
                turn_tiles(B0, xn, ln_xT)
                pe.wait_ge(ln_xTs, [1, 2, 4, 5][u])

            xTn = xT[:, HALO:HALO + N]

            def up(u, e):
                k = u * E + e
                if e >= 2:
                    pe.wait_ge(f_h, HH * (k - 1))
                for m in range(HH):
                    o = bank[3 + 2 * (e % 2) + m][:, :]
                    c = slice(m * P, (m + 1) * P)
                    pe.matmul(o, W1h[:, e, c], xh[:, :], start=True, stop=False)
                    pe.matmul(o, W1h[:, e, c], xl[:, :], start=False, stop=False)
                    pe.matmul(o, W1l[:, e, c], xh[:, :], start=False, stop=True).then_inc(f_up, 1)

            def down(u, e):
                k = u * E + e
                pe.wait_ge(f_h, HH * (k + 1))
                if e >= 2:
                    pe.wait_ge(f_acc, k - 1)
                for t in range(NT):
                    for m in range(HH):
                        mm = pe.matmul(tile(bank[1 + e % 2], t), tile(h[:, e % 2, m, :], t), W2[:, e, m, :],
                                       start=m == 0, stop=m == HH - 1)
                mm.then_inc(f_dn, 1)

            def moe(u, norm):
                norm_T(norm)
                for t in range(NT):
                    o = B1[:, t * E:(t + 1) * E]
                    pe.matmul(o, tile(xTn, t), Wr[:, :], start=True, stop=False)
                    mm = pe.matmul(o, ones[:, :], brow[:, :], start=False, stop=True)
                mm.then_inc(f_lg, 1)
                pe.wait_ge(ln_xTs, [3, 6][u])
                pe.wait_ge(xl_ready, u + 1)
                if u == 0:
                    pe.wait_ge(w1_split, 2)
                    pe.wait_ge(l_w2, 64)
                up(u, 0)
                pe.wait_ge(f_comb, u + 1)
                for t in range(NT):
                    mm = pe.transpose(B2[0:E, t * P:(t + 1) * P], comb[:, t, :], ident[:, :])
                mm.then_inc(f_cT, 1)
                up(u, 1)
                pe.wait_ge(f_cTs, u + 1)
                for t in range(NT):
                    mm = pe.matmul(tile(B0, t), tile(cT, t), b2r[:, :], start=True, stop=True)
                mm.then_inc(f_b2, 1)
                for e in range(E):
                    down(u, e)
                    if e + 2 < E:
                        up(u, e + 2)

            with pe.Fori(0, NB) as b:
                norm_T(0)
                pe.matmul(B1[:, :], Wq[:, :], xTn, start=True, stop=True).then_inc(a_proj, 1)
                pe.matmul(B2[:, :], Wk[:, :], xTn, start=True, stop=True).then_inc(a_proj, 1)
                pe.matmul(B3[0:AD, :], G1[:, :], xTn, start=True, stop=True).then_inc(a_proj, 1)
                for t in range(NT):
                    mm = pe.matmul(tile(B4, t), tile(xTn, t), Wv[:, :], start=True, stop=True)
                mm.then_inc(a_proj, 1)
                pe.wait_ge(a_g1s, 1)
                for t in range(NT):
                    mm = pe.matmul(tile(B5, t), tile(g1T, t), G2[:, :], start=True, stop=True)
                mm.then_inc(a_gate, 1)
                pe.wait_ge(a_qk, 1)
                pe.wait_ge(a_qkv, 1)
                for hd in range(AH):
                    r = slice(hd * AD, (hd + 1) * AD)
                    for t in range(NT):
                        mm = pe.matmul(tile(bank[1 + hd], t), tile(k8[r, :], t), tile(q8[r, :], t), start=True, stop=True)
                mm.then_inc(a_sc, 1)
                pe.wait_ge(a_qk, 2)
                pe.wait_ge(a_vs, 1)
                for hd in range(AH):
                    r = slice(hd * AD, (hd + 1) * AD)
                    for j, (qk, w) in enumerate(((qk16, 16), (qk32, 32))):
                        for t in range(NT):
                            right = tile(qk[r, :], t).rearrange("p (k i) -> p k i", i=w)[:, :, w // 2:w]
                            c = 256 * j + 64 * t
                            mm = pe.matmul(bank[3 + hd][:, c:c + 64], tile(qk[r, :], t), right, start=True, stop=True)
                mm.then_inc(a_sc, 1)
                pe.wait_ge(a_ki, 1)
                for t in range(NT):
                    mm = pe.transpose(tile(B0, t), tile(ki, t), ident[:, :])
                mm.then_inc(a_kiT, 1)
                pe.wait_ge(a_kts, 1)
                pe.wait_ge(a_gz, 1)
                for c, bk in enumerate((B5, B6, B0, B3)):
                    r = slice(c * CH, (c + 1) * CH)
                    if c == 3:
                        pe.wait_ge(a_AT, 1)
                    for t in range(NT):
                        for hd in range(AH):
                            f = slice(hd * AD, (hd + 1) * AD)
                            mm = pe.matmul(bk[f, t * AD:(t + 1) * AD], kt[r, t, f], va[r, t, f], start=True, stop=True)
                    mm.then_inc(a_KV, 1)
                pe.wait_ge(a_ki, 2)
                for t in range(NT):
                    pe.wait_ge(a_S, 4 * t + 3)
                    for hd in range(AH):
                        f = slice(hd * AD, (hd + 1) * AD)
                        o = bank[1 + hd]
                        pe.matmul(o[:, t * AD:(t + 1) * AD], AT[:, hd, t, :], va[:, t, f], start=True, stop=False,
                                  skip_group_check=True)
                        for c in range(4):
                            n = 4 * t + c
                            mm = pe.matmul(o[c * CH:(c + 1) * CH, t * AD:(t + 1) * AD], qi[f, n * CH:(n + 1) * CH],
                                           SA[f, n, :], start=False, stop=True, skip_group_check=True)
                mm.then_inc(a_o, 1)
                pe.wait_ge(a_on, 1)
                turn_tiles(B4, og, a_oT)
                pe.wait_ge(a_oTs, 1)
                for t in range(NT):
                    mm = pe.matmul(tile(B6, t), tile(oT, t), Wo[:, :], start=True, stop=True)
                mm.then_inc(a_out, 1)
                moe(0, 1)
                norm_T(2)
                for t in range(NT):
                    o = bank[1 + t]
                    for i in range(TAPS):
                        pe.matmul(o[:, 0:CAT], xT[:, i + t * P:i + (t + 1) * P], WC[:, i, :], start=i == 0,
                                  stop=i == TAPS - 1)
                    pe.matmul(o[:, CAT:QB], tile(xTn, t), bWb[:, :], start=True, stop=True).then_inc(b_conv, 1)
                pe.wait_ge(b_v, 1)
                turn_tiles(B0, vB, b_tr)
                pe.wait_ge(b_kn, 1)
                turn_tiles(B5, kn, b_tr)
                pe.wait_ge(b_kb, 1)
                turn_tiles(B6, kb, b_tr)
                pe.wait_ge(b_q, 1)
                turn_tiles(B1, qn, b_tr)
                pe.wait_ge(b_trs, 3)
                for hd, bk in enumerate((B2, B3, B4, B5)):
                    r = slice(hd * BD, (hd + 1) * BD)
                    for t in range(NT):
                        mm = pe.matmul(tile(bk, t), tile(knT[r, :], t), tile(kbT[r, :], t), start=True, stop=True)
                    mm.then_inc(b_knk, 1)
                pe.wait_ge(b_trs, 4)
                for hd, bk in enumerate((B6, B0, B1, B2)):
                    r = slice(hd * BD, (hd + 1) * BD)
                    if hd == 3:
                        pe.wait_ge(b_BA, 1)
                    for t in range(NT):
                        mm = pe.matmul(tile(bk, t), tile(knT[r, :], t), tile(qT[r, :], t), start=True, stop=True)
                    mm.then_inc(b_loc, 1)
                for l in range(5):
                    pe.wait_ge(b_BA, BH)
                    if l:
                        pe.wait_ge(b_T, l)
                    for hd in range(BH):
                        for t in range(NT):
                            g = hd * NT + t
                            mm = pe.matmul(B3[:, g * BD:(g + 1) * BD], BA[:, hd, t, :],
                                           Tc[:, g, :] if l else idc[:, :], start=True, stop=True)
                    mm.then_inc(b_Y, 1)
                    if l:
                        pe.wait_ge(b_bd, 4 * l)
                        pe.wait_ge(b_Ys, l)
                        for g in range(G):
                            mm = pe.matmul(B4[:, g * BD:(g + 1) * BD], BDT[:, g, :], Yc[:, g, :], start=True, stop=True)
                        mm.then_inc(b_Z, 1)
                pe.wait_ge(b_bd, 20)
                pe.wait_ge(b_vk, 2)
                pe.wait_ge(b_LT, 1)
                for i, bk in enumerate((B5, B6)):
                    for t in (2 * i, 2 * i + 1):
                        for hd in range(BH):
                            c = ((t % 2) * BH + hd) * 2 * BD
                            mm = pe.matmul(bk[:, c:c + 2 * BD], BDT[:, hd * NT + t, :], VK[:, t, hd, :], start=True,
                                           stop=True)
                    mm.then_inc(b_UW, 1)
                pe.wait_ge(b_UWs, 3)
                pe.wait_ge(b_LT, 2)
                turn_tiles(B0, Wt, b_wT)
                pe.wait_ge(b_wTs, 1)
                pe.wait_ge(b_LT, BH)
                for n in range(NC):
                    t, c = n // 4, n % 4
                    r = slice(c * CH, (c + 1) * CH)
                    if n:
                        pe.wait_ge(c_S, n)
                    pe.matmul(B1[r, 0:P], wT[:, n * CH:(n + 1) * CH], Sbd[:, :], start=True, stop=True,
                              skip_group_check=True).then_inc(c_wS, 1)
                    pe.matmul(B2[r, t * P:(t + 1) * P], qT[:, n * CH:(n + 1) * CH], Sbd[:, :], start=True, stop=False,
                              skip_group_check=True)
                    pe.wait_ge(c_ua, n + 1)
                    pe.matmul(STATE[:, 0:P], kn[r, t, :], ua[r, t, :], start=False, stop=False,
                              skip_group_check=True).then_inc(c_acc, 1)
                    if c == 3:
                        for hd in range(BH):
                            f = slice(t * P + hd * BD, t * P + (hd + 1) * BD)
                            mm = pe.matmul(B2[:, f], LT[:, hd, t, :], ua[:, t, hd * BD:(hd + 1) * BD], start=False,
                                           stop=True, skip_group_check=True)
                        mm.then_inc(c_o, 1)
                pe.wait_ge(b_dls, 1)
                turn_tiles(B5, dl, b_dT)
                pe.wait_ge(b_fs, 1)
                for t in range(NT):
                    mm = pe.transpose(tile(B3, t), tile(fs, t), ident[:, :])
                mm.then_inc(b_ft, 1)
                pe.wait_ge(b_fl, 1)
                for t in range(NT):
                    mm = pe.transpose(tile(B4, t), tile(flA, t), ident[:, :])
                mm.then_inc(b_ft, 1)
                pe.wait_ge(b_dTs, 1)
                for m, bk in enumerate((B6, B0)):
                    for k, src in enumerate((xTn, fs[:, :], flA[:, :], dT[:, :])):
                        mm = pe.matmul(bk[:, :], Wf1[:, k, m * P:(m + 1) * P], src, start=k == 0, stop=k == 3)
                    mm.then_inc(b_hid, 1)
                pe.wait_ge(b_hids, HH)
                for t in range(NT):
                    o = B1[:, t * 16:(t + 1) * 16]
                    for m in range(HH):
                        pe.matmul(o, tile(hid[:, m, :], t), Wf2[:, m, :], start=m == 0, stop=False)
                    mm = pe.matmul(o, ones[:, :], bf2row[:, :], start=False, stop=True)
                mm.then_inc(b_lg, 1)
                pe.wait_ge(b_on, 1)
                turn_tiles(B5, og, b_oT)
                pe.wait_ge(b_oTs, 1)
                for t in range(NT):
                    mm = pe.matmul(tile(B6, t), tile(oT, t), bWo[:, :], start=True, stop=True)
                mm.then_inc(b_out, 1)
                moe(1, 3)
                turn_over(pe, b)

        @block.vector
        def _(dve):
            dve.memset(AT[:, :, :, :], 0.0)
            dve.memset(BDT[:, :, :], 0.0)
            dve.memset(SA[:, 0, :], 0.0)
            dve.memset(Sbd[:, :], 0.0)
            dve.memset(xT[:, 0:HALO], 0.0)
            dve.memset(vT[:, 0:VHALO], 0.0).then_inc(zeroed, 1)
            dve.wait_ge(l_b, 16 * 6)
            dve.wait_ge(s_rawTs, 1)
            for i in range(TAPS):
                if i:
                    dve.wait_ge(s_tapT, i)
                for j in range(3):
                    ins = dve.tensor_scalar(Wtap[:, j, :], WrawT[:, j, :], cw[:, j, i:i + 1], None, ALU.mult)
                ins.then_inc(s_tap, 1)
            dve.wait_ge(l_x, 16)
            dve.wait_ge(l_a, 16 * 8)
            dve.wait_ge(consts, 1)
            dve.wait_ge(l_small, 16 * N_SMALL)
            dve.wait_ge(s_itau, 1)
            dve.wait_ge(s_state0, 1)

            with dve.Fori(0, NB) as b:
                steps = [0]

                def step(ins):
                    steps[0] += 1
                    ins.then_inc(vstep, 1)
                    return steps[0]

                def settle(k=None):
                    dve.wait_ge(vstep, steps[0] if k is None else k)

                def xt(t):
                    return X[:, bass.ds(b * NT + t, 1), :].rearrange("p a d -> p (a d)")

                Xb = X[:, bass.ds(b * NT, NT), :].rearrange("p t d -> p (t d)")

                def layer_norm(u):
                    for t in range(NT):
                        k = step(dve.bn_stats(st[:, t, :], xt(t)))
                    settle()
                    for t in range(NT):
                        step(dve.bn_aggr(mv[:, t, :], st[:, t, :]))
                    settle()
                    dve.tensor_scalar(var[:, :], mv[:, :, 1], LN_EPS, None, ALU.add).then_inc(ln_var, 1)
                    dve.wait_ge(ln_rstd, u + 1)
                    for t in range(NT):
                        ins = dve.tensor_scalar(xn[:, t, :], xt(t), mv[:, t, 0:1], rstd[:, t:t + 1], ALU.subtract, ALU.mult)
                    ins.then_inc(ln_xn, 1)

                def residual(sig, bk, u):
                    dve.wait_ge(sig, 1)
                    dve.tensor_tensor(Xb, Xb, bk[:, :], ALU.add).then_inc(x_ready, 1)
                    dve.wait_ge(x_ready, u + 1)

                def rms(width, sq, u, on_sig):
                    nh = P // width * NT
                    dve.wait_ge(sq, 1)
                    step(dve.tensor_reduce(ss[:, 0:nh], flat(osq).rearrange("p (g d) -> p g d", d=width), AX, ALU.add))
                    settle()
                    dve.tensor_scalar(ss[:, 0:nh], ss[:, 0:nh], 1.0 / width, LN_EPS, ALU.mult, ALU.add).then_inc(rms_var, 1)
                    dve.wait_ge(rms_r, u)
                    v = flat(og).rearrange("p (g d) -> p g d", d=width)
                    dve.tensor_tensor(v, v, spread(ssr[:, 0:nh], width), ALU.mult).then_inc(on_sig, 1)

                def moe(u, norm):
                    layer_norm(norm)
                    dve.wait_ge(ln_xn, norm + 1)
                    step(dve.tensor_tensor(flat(acc), Xb, flat(xn), ALU.add))
                    dve.wait_ge(ln_xTs, [3, 6][u])
                    dve.tensor_tensor(xl[:, :], B0[:, :], xh[:, :], ALU.subtract).then_inc(xl_ready, 1)
                    dve.wait_ge(f_lg, u + 1)
                    step(dve.tensor_copy(lg[:, :, :].rearrange("p t e -> p (t e)"), B1[:, 0:NT * E]))
                    settle()
                    for t in range(NT):
                        step(dve.max(top[:, t, :], lg[:, t, :]))
                    settle()
                    for t in range(NT):
                        step(dve.max_index(topi[:, t, :], top[:, t, :], lg[:, t, :]))
                    dve.tensor_tensor(gap[:, :], top[:, :, 0], top[:, :, 1], ALU.subtract).then_inc(f_gap, 1)
                    settle()
                    step(dve.tensor_copy(topf[:, :, :], topi[:, :, :]))
                    dve.wait_ge(f_th, u + 1)
                    step(dve.tensor_scalar(wa[:, :], th[:, :], 0.5, 0.5, ALU.mult, ALU.add))
                    step(dve.tensor_scalar(wb[:, :], th[:, :], -0.5, 0.5, ALU.mult, ALU.add))
                    settle()
                    for t in range(NT):
                        step(dve.tensor_scalar(comb[:, t, :], iota_e[:, :], topf[:, t, 0:1], wa[:, t:t + 1],
                                               ALU.is_equal, ALU.mult))
                        step(dve.tensor_scalar(comb2[:, t, :], iota_e[:, :], topf[:, t, 1:2], wb[:, t:t + 1],
                                               ALU.is_equal, ALU.mult))
                    settle()
                    dve.tensor_tensor(comb[:, :, :], comb[:, :, :], comb2[:, :, :], ALU.add).then_inc(f_comb, 1)
                    dve.wait_ge(f_b2, u + 1)
                    step(dve.tensor_tensor(flat(acc), flat(acc), B0[:, :], ALU.add))
                    dve.wait_ge(f_comb, u + 1)
                    settle()
                    for e in range(E):
                        k = u * E + e
                        dve.wait_ge(f_dn, k + 1)
                        if e:
                            dve.wait_ge(f_acc, k)
                        for t in range(NT):
                            ins = dve.scalar_tensor_tensor(acc[:, t, :], tile(bank[1 + e % 2], t), comb[:, t, e:e + 1],
                                                           acc[:, t, :], ALU.mult, ALU.add)
                        ins.then_inc(f_acc, 1)
                    dve.wait_ge(f_acc, (u + 1) * E)
                    dve.tensor_copy(Xb, flat(acc)).then_inc(x_ready, 1)
                    dve.wait_ge(x_ready, norm + 1)

                layer_norm(0)
                dve.wait_ge(a_proj, 1)
                dve.tensor_scalar(qc[:, :], B1[:, :], EXP_MIN, None, ALU.max).then_inc(a_qc, 1)
                dve.wait_ge(a_proj, 2)
                dve.tensor_scalar(z[:, :], B2[:, :], deltac[:, :], Z_MIN, ALU.add, ALU.max).then_inc(a_z, 1)
                dve.wait_ge(a_eq, 1)
                dve.wait_ge(a_ez, 1)
                step(dve.tensor_scalar(eq[:, :], eq[:, :], 1.0, None, ALU.add))
                step(dve.tensor_copy(ks[:, :], ez[:, :]))
                settle()
                dve.tensor_scalar(ez[:, :], ez[:, :], 1.0, None, ALU.add).then_inc(a_ez1, 1)
                step(dve.reciprocal(rq[:, :], eq[:, :]))
                dve.wait_ge(a_ez1, 1)
                step(dve.reciprocal(rz[:, :], ez[:, :]))
                settle(steps[0] - 1)
                dve.tensor_tensor(qs[:, :], B1[:, :], rq[:, :], ALU.mult).then_inc(a_qkv, 1)
                settle()
                dve.tensor_tensor(ks[:, :], ks[:, :], rz[:, :], ALU.mult).then_inc(a_k, 1)
                dve.wait_ge(a_lnf, 1)
                step(dve.tensor_scalar(lnf[:, :], lnf[:, :], MAX_DECAY, None, ALU.min))
                settle()
                dve.tensor_tensor_scan(H[:, :], scan_on[:, :], lnf[:, :], 0.0, ALU.mult, ALU.add).then_inc(a_H, 1)
                dve.wait_ge(a_H, 1)

                def against(dst, width, ref, sig):
                    Hv = H[:, :].rearrange("p (k i) -> p k i", i=width)
                    dv = dst[:, :].rearrange("p (k i) -> p k i", i=width)
                    half = width // 2
                    at = Hv[:, :, ref:ref + 1].broadcast_to([P, N // width, half])
                    dve.tensor_tensor(dv[:, :, half:], Hv[:, :, half:], at, ALU.subtract).then_inc(sig, 1)
                    dve.tensor_tensor(dv[:, :, :half], at, Hv[:, :, :half], ALU.subtract).then_inc(sig, 1)

                H8 = H[:, :].rearrange("p (k i) -> p k i", i=8)
                dve.tensor_tensor(D8[:, :].rearrange("p (k i) -> p k i", i=8), H8,
                                  H8[:, :, 3:4].broadcast_to([P, N // 8, 8]), ALU.subtract).then_inc(a_D8, 1)
                against(D16, 16, 7, a_D16)
                HC = H[:, :].rearrange("p (k i) -> p k i", i=CH)
                dve.tensor_tensor(DT[:, :].rearrange("p (k i) -> p k i", i=CH),
                                  HC[:, :, CH - 1:CH].broadcast_to([P, NC, CH]), HC, ALU.subtract).then_inc(a_DT, 1)
                against(D32, 32, 15, a_D32)
                dve.wait_ge(a_gate, 1)
                dve.tensor_scalar(flat(sg), B5[:, :], EXP_MIN, None, ALU.max).then_inc(a_gz, 1)
                dve.wait_ge(a_exps, 4)
                dve.wait_ge(a_qkv, 1)
                dve.wait_ge(a_k, 1)
                dve.tensor_tensor(q8[:, :], qs[:, :], E8q[:, :], ALU.mult)
                dve.tensor_tensor(k8[:, :], ks[:, :], E8k[:, :], ALU.mult).then_inc(a_qk, 1)
                dve.wait_ge(a_exps, 7)
                for dst, ex, w in ((qk16, E16, 16), (qk32, E32, 32)):
                    d, s, q_, k_ = (y[:, :].rearrange("p (k i) -> p k i", i=w) for y in (dst, ex, qs, ks))
                    dve.tensor_tensor(d[:, :, w // 2:], q_[:, :, w // 2:], s[:, :, w // 2:], ALU.mult)
                    ins = dve.tensor_tensor(d[:, :, :w // 2], k_[:, :, :w // 2], s[:, :, :w // 2], ALU.mult)
                ins.then_inc(a_qk, 1)
                dve.wait_ge(a_eg, 1)
                step(dve.tensor_scalar(flat(sg), flat(sg), 1.0, None, ALU.add))
                settle()
                step(dve.reciprocal(flat(sg), flat(sg)))
                dve.wait_ge(a_sc, 1)
                for hd in range(AH):
                    step(dve.copy_predicated(AT[:, hd, :, :].rearrange("p t i -> p (t i)"), flat(m8).bitcast(I32),
                                             bank[1 + hd][:, :]))
                settle()
                dve.wait_ge(a_sc, 2)
                for j, (m, w) in enumerate(((m16, 16), (m32, 32))):
                    for hd in range(AH):
                        dst = AT[:, hd, :, :].rearrange("p t (k i) -> p (t k) i", i=w)[:, :, w // 2:]
                        src = bank[3 + hd][:, 256 * j:256 * (j + 1)].rearrange("p (k i) -> p k i", i=w // 2)
                        ins = dve.copy_predicated(dst, m[:, :, :].bitcast(I32), src)
                        if j == 0:
                            step(ins)
                    if j == 0:
                        settle()
                ins.then_inc(a_AT, 1)
                for n in range(NC):
                    t, c = n // 4, n % 4
                    if n < 4:
                        dve.wait_ge(a_KV, n + 1)
                    if n:
                        dve.wait_ge(a_S, n)
                    dve.scalar_tensor_tensor(SA[:, n + 1, :], SA[:, n, :], Fd[:, n:n + 1],
                                             (B5, B6, B0, B3)[c][:, t * AD:(t + 1) * AD], ALU.mult, ALU.add).then_inc(a_S, 1)
                dve.wait_ge(a_o, 1)
                settle()
                for hd in range(AH):
                    f = slice(hd * AD, (hd + 1) * AD)
                    ins = dve.tensor_tensor(og[:, :, f], bank[1 + hd][:, 0:NT * AD].rearrange("p (t d) -> p t d", d=AD),
                                            sg[:, :, f], ALU.mult)
                ins.then_inc(a_og, 1)
                dve.wait_ge(a_S, NC)
                dve.tensor_copy(SA[:, 0, :], SA[:, NC, :])
                rms(AD, a_osq, 1, a_on)
                residual(a_out, B6, 0)

                moe(0, 1)

                layer_norm(2)
                for t in range(NT):
                    dve.wait_ge(b_th, t + 1)
                    dve.scalar_tensor_tensor(s2[:, t, :], thB[:, t, 0:CAT], 1.0, bank[1 + t][:, 0:CAT], ALU.add,
                                             ALU.mult).then_inc(b_s2, 1)
                step(dve.tensor_scalar(beta[:, :, :], thB[:, :, CAT:QB], 0.5, 0.5, ALU.mult, ALU.add))
                dve.wait_ge(b_sq, 1)
                step(dve.tensor_reduce(ss[:, 0:32], s2q[:, :, :].rearrange("p t (g d) -> p (t g) d", d=BD), AX, ALU.add))
                settle()
                dve.tensor_scalar(ss[:, 0:32], ss[:, 0:32], 4e-6, None, ALU.add).then_inc(b_ss, 1)
                bet = spread(beta[:, :, :].rearrange("p t h -> p (t h)"), BD)
                dve.wait_ge(b_v, 1)
                vk = VK[:, :, :, :].rearrange("p t h c -> p (t h) c")
                dve.tensor_tensor(vk[:, :, 0:BD], heads(vB), bet, ALU.mult).then_inc(b_vk, 1)
                dve.wait_ge(b_rn, 1)
                rn = ssr[:, :].rearrange("p (t g) -> p t g", g=2 * BH)
                for t in range(NT):
                    ins = dve.tensor_tensor(kn[:, t, :].rearrange("p (h d) -> p h d", d=BD),
                                            s2[:, t, P:2 * P].rearrange("p (h d) -> p h d", d=BD),
                                            spread(rn[:, t, BH:2 * BH], BD), ALU.mult)
                ins.then_inc(b_kn, 1)
                dve.wait_ge(b_kn, 1)
                dve.tensor_tensor(heads(kb), heads(kn), bet, ALU.mult).then_inc(b_kb, 1)
                dve.wait_ge(b_kb, 1)
                dve.tensor_copy(vk[:, :, BD:2 * BD], heads(kb)).then_inc(b_vk, 1)
                for t in range(NT):
                    ins = dve.tensor_tensor(qn[:, t, :].rearrange("p (h d) -> p h d", d=BD),
                                            s2[:, t, 0:P].rearrange("p (h d) -> p h d", d=BD),
                                            spread(rn[:, t, 0:BH], BD), ALU.mult)
                ins.then_inc(b_q, 1)
                for hd, bk in enumerate((B2, B3, B4, B5)):
                    dve.wait_ge(b_knk, hd + 1)
                    dve.tensor_tensor(BA[:, hd, :, :].rearrange("p t i -> p (t i)"), bk[:, :], flat(upneg),
                                      ALU.mult).then_inc(b_BA, 1)
                step(dve.tensor_copy(Tc[:, :, :], idc[:, :].unsqueeze(1).broadcast_to([P, G, BD])))
                for l in range(5):
                    dve.wait_ge(b_Z if l else b_Y, max(l, 1))
                    settle()
                    step(dve.copy_predicated(Tc[:, :, :],
                                             lev[:, l, :].bitcast(I32).unsqueeze(1).broadcast_to([P, G, BD]),
                                             (B4 if l else B3)[:, :].rearrange("p (g i) -> p g i", i=BD)))
                    settle()
                    if l:
                        dve.wait_ge(b_bd, 4 * l)
                    dve.transpose(TTc[:, :, :].rearrange("p g i -> p (g i)"),
                                  Tc[:, :, :].rearrange("p g i -> p (g i)")).then_inc(b_T, 1)
                    dve.wait_ge(b_T, l + 1)
                    if l:
                        dve.wait_ge(b_Z, l)
                    for c in (2, 3):
                        dve.tensor_copy(BDT[c * CH:(c + 1) * CH, :, c * CH:(c + 1) * CH],
                                        TTc[c * CH:(c + 1) * CH, :, :]).then_inc(b_bd, 1)
                for hd, bk in enumerate((B6, B0, B1, B2)):
                    dve.wait_ge(b_loc, hd + 1)
                    dve.tensor_tensor(LT[:, hd, :, :].rearrange("p t i -> p (t i)"), bk[:, :], flat(upinc),
                                      ALU.mult).then_inc(b_LT, 1)
                dve.wait_ge(b_trs, 1)
                written = {}

                def fir_tap(j):
                    if j >= FS + FL:
                        return
                    if j < 3 * FS and j % 3 == 0:
                        name, dst, w, i, n = "short", fs, firs, j // 3, FS
                    else:
                        i = j - min(j // 3 + 1, FS)
                        name, dst, w, n = ("even", flA, firl, FL) if i % 2 == 0 else ("odd", flB, firl, FL)
                    src = vT[:, VHALO - (n - 1) + i:VHALO - (n - 1) + i + N]
                    if name not in written:
                        written[name] = step(dve.tensor_scalar(dst, src, w[:, i:i + 1], None, ALU.mult))
                        return
                    settle(written[name])
                    ins = dve.scalar_tensor_tensor(dst, src, w[:, i:i + 1], dst, ALU.mult, ALU.add)
                    if name == "short" and i == FS - 1:
                        ins.then_inc(b_fs, 1)
                    else:
                        written[name] = step(ins)

                dve.wait_ge(b_UWs, 4)
                for n in range(NC):
                    t, c = n // 4, n % 4
                    r = slice(c * CH, (c + 1) * CH)
                    dve.wait_ge(c_wS, n + 1)
                    dve.tensor_tensor(ua[r, t, :], U[r, t, :], B1[r, 0:P], ALU.subtract).then_inc(c_ua, 1)
                    fir_tap(2 * n)
                    dve.wait_ge(c_acc, n + 1)
                    dve.tensor_tensor(Sbd[:, :], STATE[:, 0:P], same[:, :], ALU.mult).then_inc(c_S, 1)
                    fir_tap(2 * n + 1)
                for j in range(2 * NC, FS + FL):
                    fir_tap(j)
                settle()
                dve.tensor_tensor(flA[:, :], flA[:, :], flB[:, :], ALU.add).then_inc(b_fl, 1)
                dve.wait_ge(b_lg, 1)
                dve.tensor_copy(l2[:, :, :, :].rearrange("p t h c -> p (t h c)"), B1[:, 0:NT * 16]).then_inc(b_l3, 1)
                dve.wait_ge(b_l3, 1)
                lv = l2[:, :, :, :].rearrange("p t h c -> p (t h) c")
                lsv = ls[:, :, :, :].rearrange("p t h c -> p (t h) c")
                for t in range(NT):
                    step(dve.tensor_tensor(ls[:, t, :, :], l2[:, t, :, 0:3], spread(itau[:, :], 3), ALU.mult))
                settle()
                lm = lsm[:, :, :].rearrange("p t h -> p (t h)")
                step(dve.tensor_reduce(lm, lsv, AX, ALU.max))
                settle()
                dve.tensor_tensor(lsv, lsv, spread(lm, 3), ALU.subtract).then_inc(b_lsm, 1)
                dve.wait_ge(b_t3, 1)
                step(dve.tensor_scalar(pr[:, :, :], t3[:, :, :], 0.5, 0.5, ALU.mult, ALU.add))
                settle()
                step(dve.tensor_scalar(pv[:, :, :], pr[:, :, :], 0.09, 0.9, ALU.mult, ALU.add))
                settle()
                step(dve.tensor_tensor(pv[:, :, :], pv[:, :, :], pr[:, :, :], ALU.mult))
                dve.wait_ge(b_pe, 1)
                pex = pe_[:, :, :, :].rearrange("p t h c -> p (t h) c")
                rsv = rs_[:, :, :].rearrange("p t h -> p (t h)")
                step(dve.tensor_reduce(rsv, pex, AX, ALU.add))
                settle()
                step(dve.reciprocal(rsv, rsv))
                step(dve.tensor_scalar(cc[:, :, :], pv[:, :, :], -1.0, 1.0, ALU.mult, ALU.add))
                settle()
                step(dve.tensor_tensor(cc[:, :, :], cc[:, :, :], rs_[:, :, :], ALU.mult))
                settle()
                pcv = pc[:, :, :, :].rearrange("p t h c -> p (t h) c")
                step(dve.tensor_tensor(pcv, pex, spread(cc[:, :, :].rearrange("p t h -> p (t h)"), 3), ALU.mult))
                settle()
                dve.wait_ge(b_ft, 2)
                b3v, b4v = (bk[:, :].rearrange("p (g d) -> p g d", d=BD) for bk in (B3, B4))
                step(dve.tensor_tensor(heads(m1_), b3v, spread(pcv[:, :, 0], BD), ALU.mult))
                step(dve.tensor_tensor(heads(m2_), b4v, spread(pcv[:, :, 1], BD), ALU.mult))
                step(dve.tensor_tensor(heads(m3_), heads(dl), spread(pcv[:, :, 2], BD), ALU.mult))
                step(dve.tensor_tensor(heads(m4_), heads(vB), spread(pv[:, :, :].rearrange("p t h -> p (t h)"), BD),
                                       ALU.mult))
                settle()
                step(dve.tensor_tensor(flat(m1_), flat(m1_), flat(m2_), ALU.add))
                step(dve.tensor_tensor(flat(m3_), flat(m3_), flat(m4_), ALU.add))
                settle()
                dve.tensor_tensor(flat(og), flat(m1_), flat(m3_), ALU.add).then_inc(b_mix, 1)
                rms(BD, b_osq, 2, b_on)
                residual(b_out, B6, 2)

                moe(1, 3)
                turn_over(dve, b)


_INS = ['L0_attn_a_x', 'L0_attn_a_Wq', 'L0_attn_a_Wk', 'L0_attn_a_Wv', 'L0_attn_a_Wo', 'L0_attn_a_delta', 'L0_attn_a_G1',
        'L0_attn_a_G2', 'L0_attn_a_norm_w', 'L0_attn_b_W_q', 'L0_attn_b_W_k', 'L0_attn_b_W_v', 'L0_attn_b_W_b',
        'L0_attn_b_conv_w_q', 'L0_attn_b_conv_w_k', 'L0_attn_b_conv_w_v', 'L0_attn_b_fir_short_w', 'L0_attn_b_fir_long_w',
        'L0_attn_b_W_fuse1', 'L0_attn_b_b_fuse1', 'L0_attn_b_W_fuse2', 'L0_attn_b_b_fuse2', 'L0_attn_b_others_log_tau',
        'L0_attn_b_norm_w', 'L0_attn_b_W_o', 'L0_ffn_Wr', 'L0_ffn_br', 'L0_ffn_W1', 'L0_ffn_b1', 'L0_ffn_W2', 'L0_ffn_b2']


def kernel(**inputs):
    import numpy as _np
    import concourse.bacc as _bacc
    from concourse import mybir as _mybir
    from concourse.bass_utils import run_bass_kernel_spmd as _run

    nc = _bacc.Bacc("TRN2", target_bir_lowering=False, num_devices=1)
    arrays, args = {}, []
    for name in _INS:
        a = _np.ascontiguousarray(inputs[name])
        arrays[f"in_{name}"] = a
        args.append(nc.dram_tensor(f"in_{name}", a.shape, _mybir.dt.from_np(a.dtype), kind="ExternalInput").ap())
    shape = inputs['L0_attn_a_x'].shape
    args.append(nc.dram_tensor("out_0", shape, _mybir.dt.float32, kind="ExternalOutput").ap())
    hybrid_kernel(nc, *args)
    r = _run(nc, [arrays], core_ids=[0])
    return r.results[0]["out_0"]
```
